# Optimizing a Trainium2 kernel written in Bass

```python
import numpy as np
import jax
import jax.numpy as jnp

def _softmax(x, axis=-1):
    return jax.nn.softmax(x, axis=axis)

def _gelu(x):
    return jax.nn.gelu(x, approximate=True)

def _silu(x):
    return jax.nn.silu(x)

def _sigmoid(x):
    return jax.nn.sigmoid(x)

def _layernorm(x, axis=-1, eps=1e-05):
    m = jnp.mean(x, axis=axis, keepdims=True)
    v = jnp.var(x, axis=axis, keepdims=True)
    return (x - m) / jnp.sqrt(v + eps)

def _scatter_add(tgt, idx, src, axis=0):
    return tgt.at[idx].add(src)

def _segment_sum(src, seg, n):
    return jax.ops.segment_sum(src, seg, n)
kernel_name = 'mk_dlrm_tower_d1_rec_r8_f1ec52'

def setup_inputs(seed: int=0):
    np.random.seed(seed)
    _w = jnp.asarray

    def _rec_inputs():
        import jax
        import jax.numpy as jnp
        _tk = jax.random.key(seed)
        dense_ctx = jax.random.normal(jax.random.fold_in(_tk, 190), (512, 16), jnp.float32)
        ids = jnp.stack([jax.random.randint(jax.random.fold_in(_tk, 200 + f), (512,), 0, v, jnp.int32) for f, v in enumerate([1000, 1250, 125000, 1000, 1000, 12500, 1000, 1000, 1000, 12500, 1250, 1000, 1250, 12500, 12500, 1000, 1000, 1000, 1250, 12500, 1000, 1250, 1000, 1250, 12500, 1250, 1250])], axis=1)
        tbl_0 = 0.05 * jax.random.normal(jax.random.fold_in(_tk, 500 + 0), (1000, 128), jnp.float32)
        tbl_1 = 0.05 * jax.random.normal(jax.random.fold_in(_tk, 500 + 1), (1250, 128), jnp.float32)
        tbl_2 = 0.05 * jax.random.normal(jax.random.fold_in(_tk, 500 + 2), (125000, 128), jnp.float32)
        tbl_3 = 0.05 * jax.random.normal(jax.random.fold_in(_tk, 500 + 3), (1000, 128), jnp.float32)
        tbl_4 = 0.05 * jax.random.normal(jax.random.fold_in(_tk, 500 + 4), (1000, 128), jnp.float32)
        tbl_5 = 0.05 * jax.random.normal(jax.random.fold_in(_tk, 500 + 5), (12500, 128), jnp.float32)
        tbl_6 = 0.05 * jax.random.normal(jax.random.fold_in(_tk, 500 + 6), (1000, 128), jnp.float32)
        tbl_7 = 0.05 * jax.random.normal(jax.random.fold_in(_tk, 500 + 7), (1000, 128), jnp.float32)
        tbl_8 = 0.05 * jax.random.normal(jax.random.fold_in(_tk, 500 + 8), (1000, 128), jnp.float32)
        tbl_9 = 0.05 * jax.random.normal(jax.random.fold_in(_tk, 500 + 9), (12500, 128), jnp.float32)
        tbl_10 = 0.05 * jax.random.normal(jax.random.fold_in(_tk, 500 + 10), (1250, 128), jnp.float32)
        tbl_11 = 0.05 * jax.random.normal(jax.random.fold_in(_tk, 500 + 11), (1000, 128), jnp.float32)
        tbl_12 = 0.05 * jax.random.normal(jax.random.fold_in(_tk, 500 + 12), (1250, 128), jnp.float32)
        tbl_13 = 0.05 * jax.random.normal(jax.random.fold_in(_tk, 500 + 13), (12500, 128), jnp.float32)
        tbl_14 = 0.05 * jax.random.normal(jax.random.fold_in(_tk, 500 + 14), (12500, 128), jnp.float32)
        tbl_15 = 0.05 * jax.random.normal(jax.random.fold_in(_tk, 500 + 15), (1000, 128), jnp.float32)
        tbl_16 = 0.05 * jax.random.normal(jax.random.fold_in(_tk, 500 + 16), (1000, 128), jnp.float32)
        tbl_17 = 0.05 * jax.random.normal(jax.random.fold_in(_tk, 500 + 17), (1000, 128), jnp.float32)
        tbl_18 = 0.05 * jax.random.normal(jax.random.fold_in(_tk, 500 + 18), (1250, 128), jnp.float32)
        tbl_19 = 0.05 * jax.random.normal(jax.random.fold_in(_tk, 500 + 19), (12500, 128), jnp.float32)
        tbl_20 = 0.05 * jax.random.normal(jax.random.fold_in(_tk, 500 + 20), (1000, 128), jnp.float32)
        tbl_21 = 0.05 * jax.random.normal(jax.random.fold_in(_tk, 500 + 21), (1250, 128), jnp.float32)
        tbl_22 = 0.05 * jax.random.normal(jax.random.fold_in(_tk, 500 + 22), (1000, 128), jnp.float32)
        tbl_23 = 0.05 * jax.random.normal(jax.random.fold_in(_tk, 500 + 23), (1250, 128), jnp.float32)
        tbl_24 = 0.05 * jax.random.normal(jax.random.fold_in(_tk, 500 + 24), (12500, 128), jnp.float32)
        tbl_25 = 0.05 * jax.random.normal(jax.random.fold_in(_tk, 500 + 25), (1250, 128), jnp.float32)
        tbl_26 = 0.05 * jax.random.normal(jax.random.fold_in(_tk, 500 + 26), (1250, 128), jnp.float32)
        _rk = jax.random.fold_in(_tk, 7)
        W_top1 = 0.0521996 * jax.random.normal(jax.random.fold_in(_tk, 801), (367, 512), jnp.float32)
        W_top2 = 0.0441942 * jax.random.normal(jax.random.fold_in(_tk, 802), (512, 256), jnp.float32)
        W_top3 = 0.0625 * jax.random.normal(jax.random.fold_in(_tk, 803), (256, 1), jnp.float32)
        b_top1 = jnp.zeros((512,), jnp.float32)
        b_top2 = jnp.zeros((256,), jnp.float32)
        return (dense_ctx, ids, tbl_0, tbl_1, tbl_2, tbl_3, tbl_4, tbl_5, tbl_6, tbl_7, tbl_8, tbl_9, tbl_10, tbl_11, tbl_12, tbl_13, tbl_14, tbl_15, tbl_16, tbl_17, tbl_18, tbl_19, tbl_20, tbl_21, tbl_22, tbl_23, tbl_24, tbl_25, tbl_26, W_top1, b_top1, W_top2, b_top2, W_top3)
    dense_ctx, ids, tbl_0, tbl_1, tbl_2, tbl_3, tbl_4, tbl_5, tbl_6, tbl_7, tbl_8, tbl_9, tbl_10, tbl_11, tbl_12, tbl_13, tbl_14, tbl_15, tbl_16, tbl_17, tbl_18, tbl_19, tbl_20, tbl_21, tbl_22, tbl_23, tbl_24, tbl_25, tbl_26, W_top1, b_top1, W_top2, b_top2, W_top3 = _rec_inputs()

    def _L0_rec_setup():
        import jax, jax.numpy as jnp
        import numpy as np

        def _tri_indices(num_feas):
            return np.array([i * num_feas + j for j in range(1, num_feas) for i in range(j)], dtype=np.int32)
        key = jax.random.key(seed)
        batch, num_feas, embed_dim = (2048, 27, 128)
        inputs = jax.random.normal(key, (batch, num_feas, embed_dim), dtype=jnp.float32)
        return {'inputs': inputs, 'num_feas': num_feas}
    _L0_rec_all = _L0_rec_setup()
    _L0_rec_in = {k: v for k, v in _L0_rec_all.items() if k in ()}
    del _L0_rec_all
    return {'dense_ctx': dense_ctx, 'ids': ids, 'tbl_0': tbl_0, 'tbl_1': tbl_1, 'tbl_2': tbl_2, 'tbl_3': tbl_3, 'tbl_4': tbl_4, 'tbl_5': tbl_5, 'tbl_6': tbl_6, 'tbl_7': tbl_7, 'tbl_8': tbl_8, 'tbl_9': tbl_9, 'tbl_10': tbl_10, 'tbl_11': tbl_11, 'tbl_12': tbl_12, 'tbl_13': tbl_13, 'tbl_14': tbl_14, 'tbl_15': tbl_15, 'tbl_16': tbl_16, 'tbl_17': tbl_17, 'tbl_18': tbl_18, 'tbl_19': tbl_19, 'tbl_20': tbl_20, 'tbl_21': tbl_21, 'tbl_22': tbl_22, 'tbl_23': tbl_23, 'tbl_24': tbl_24, 'tbl_25': tbl_25, 'tbl_26': tbl_26, 'W_top1': W_top1, 'b_top1': b_top1, 'W_top2': W_top2, 'b_top2': b_top2, 'W_top3': W_top3}

def reference(dense_ctx, ids, tbl_0, tbl_1, tbl_2, tbl_3, tbl_4, tbl_5, tbl_6, tbl_7, tbl_8, tbl_9, tbl_10, tbl_11, tbl_12, tbl_13, tbl_14, tbl_15, tbl_16, tbl_17, tbl_18, tbl_19, tbl_20, tbl_21, tbl_22, tbl_23, tbl_24, tbl_25, tbl_26, W_top1, b_top1, W_top2, b_top2, W_top3):
    import jax
    import jax.numpy as jnp

    def _L0_rec_ref(inputs, num_feas):
        import jax, jax.numpy as jnp
        import numpy as np

        def _tri_indices(num_feas):
            return np.array([i * num_feas + j for j in range(1, num_feas) for i in range(j)], dtype=np.int32)
        dot = jnp.einsum('bnd,bmd->bnm', inputs, inputs)
        idx = jnp.asarray(_tri_indices(num_feas))
        flat = dot.reshape(inputs.shape[0], num_feas * num_feas)
        return flat[:, idx]
    e = jnp.stack([tbl_0[ids[:, 0]], tbl_1[ids[:, 1]], tbl_2[ids[:, 2]], tbl_3[ids[:, 3]], tbl_4[ids[:, 4]], tbl_5[ids[:, 5]], tbl_6[ids[:, 6]], tbl_7[ids[:, 7]], tbl_8[ids[:, 8]], tbl_9[ids[:, 9]], tbl_10[ids[:, 10]], tbl_11[ids[:, 11]], tbl_12[ids[:, 12]], tbl_13[ids[:, 13]], tbl_14[ids[:, 14]], tbl_15[ids[:, 15]], tbl_16[ids[:, 16]], tbl_17[ids[:, 17]], tbl_18[ids[:, 18]], tbl_19[ids[:, 19]], tbl_20[ids[:, 20]], tbl_21[ids[:, 21]], tbl_22[ids[:, 22]], tbl_23[ids[:, 23]], tbl_24[ids[:, 24]], tbl_25[ids[:, 25]], tbl_26[ids[:, 26]]], axis=1)
    z = _L0_rec_ref(e, 27)
    z = z.reshape(z.shape[0], -1)
    h = jnp.concatenate([z, dense_ctx], axis=1)
    h = jnp.maximum(h @ W_top1 + b_top1, 0.0)
    h = jnp.maximum(h @ W_top2 + b_top2, 0.0)
    y = h @ W_top3
    return y

_drawn_inputs = setup_inputs


def setup_inputs(seed=0):
    import zlib

    import numpy as np

    out = dict(_drawn_inputs(seed))
    spreads = {'b_top1': (0.0, 0.1), 'b_top2': (0.0, 0.1)}
    factors = {}
    for name, (base, spread) in spreads.items():
        noise = np.random.default_rng([zlib.crc32(name.encode()), seed]).standard_normal(out[name].shape)
        drawn = base * np.exp(spread * noise) if base else spread * noise
        out[name] = jnp.asarray(drawn.astype(out[name].dtype))
    for name, factor in factors.items():
        out[name] = (out[name] * factor).astype(out[name].dtype)
    return out
```

```python
from contextlib import ExitStack

import concourse.bass as bass
from concourse import mybir

P = 128
QUAD = 32


def dlrm_tower_kernel(nc, dense_t, ids, tables, w1, b1, w2, b2, w3, out):
    F32, I32 = mybir.dt.float32, mybir.dt.int32
    ALU, ACT = mybir.AluOpType, mybir.ActivationFunctionType

    NF = len(tables)
    D = tables[0].shape[1]
    NDENSE, B = dense_t.shape
    H1, H2 = w2.shape
    CHUNKS = B // P
    NPAIR = NF * (NF - 1) // 2
    assert D == P and NF <= QUAD and w1.shape[0] == NPAIR + NDENSE
    T1, T2 = H1 // P, H2 // P

    TG = 4
    NG = -(-NF // TG)
    GROUP = [list(range(g * TG, min(NF, g * TG + TG))) for g in range(NG)]
    SQ = P // QUAD
    NQ = P // SQ
    FILLG = 8
    FILLS = NQ // FILLG
    JJ = -(-(NF - 1) // SQ)
    COLS = [[j for j in range(1 + q * JJ, min(NF, 1 + q * JJ + JJ))] for q in range(SQ)]
    DENSE_Q, DENSE_JJ = SQ - 1, len(COLS[SQ - 1])
    assert DENSE_JJ < JJ
    USED = [sum(1 for q in range(SQ) if jj < len(COLS[q]) or (q, jj) == (DENSE_Q, DENSE_JJ)) * QUAD
            for jj in range(JJ)]

    with ExitStack() as ctx:
        def sb(name, shape, dt=F32):
            return ctx.enter_context(nc.sbuf_tensor(name, shape, dt))

        def psum(name, shape):
            return ctx.enter_context(nc.psum_tensor(name, shape, F32))

        def sem(name):
            return ctx.enter_context(nc.semaphore(name))

        ids_sb = sb("ids_sb", [P, CHUNKS * NF], I32)
        ident = sb("ident", [P, P])
        rows = sb("rows", [P, NF, D])
        rows_t = sb("rows_t", [P, P, QUAD])
        pairs = sb("pairs", [P, JJ, P])
        w1_sb = sb("w1_sb", [P, JJ, H1])
        w2_sb = sb("w2_sb", [P, T1, H2])
        w3_sb = sb("w3_sb", [P, T2])
        b1_sb = sb("b1_sb", [P, T1])
        b2_sb = sb("b2_sb", [P, T2])
        dense_sb = sb("dense_sb", [P, B])
        h1_sb = sb("h1_sb", [P, T1, P])
        h2_sb = sb("h2_sb", [P, T2, P])
        y_sb = sb("y_sb", [1, B])

        turned_ps = [psum(f"turned_ps{i}", [P, TG, P]) for i in range(2)]
        prod_ps = [psum(f"prod_ps{i}", [P, FILLG, P]) for i in range(2)]
        mlp_ps = [psum("mlp_ps_dve", [P, 4, P]), psum("mlp_ps_act", [P, 4, P])]
        HALF = T1 // 2
        assert HALF == T2 == 2

        def h1_ps(t):
            return mlp_ps[t // HALF][:, t % HALF, :]

        def h2_ps(u):
            return mlp_ps[u][:, HALF, :]

        y_ps = mlp_ps[0][0:1, HALF + 1, :]

        ids_in = sem("ids_in")
        weights_in = sem("weights_in")
        small_in = sem("small_in")
        dense_in = sem("dense_in")
        w1_cleared = sem("w1_cleared")
        ident_zero = sem("ident_zero")
        ident_ready = sem("ident_ready")
        pads_ready = sem("pads_ready")
        gathered = [sem(f"gathered{g}") for g in range(NG)]
        turned = sem("turned")
        dve_rows_t = sem("dve_rows_t")
        act_rows_t = sem("act_rows_t")
        products = sem("products")
        dve_pairs = sem("dve_pairs")
        act_pairs = sem("act_pairs")
        dense_placed = sem("dense_placed")
        layer1 = sem("layer1")
        dve_h1 = sem("dve_h1")
        act_h1 = sem("act_h1")
        layer2 = sem("layer2")
        dve_h2 = sem("dve_h2")
        act_h2 = sem("act_h2")
        layer3 = sem("layer3")
        y_copied = sem("y_copied")
        y_out = sem("y_out")

        DVE_G = [g for g in range(NG) if g % 2 == 0]
        ACT_G = [g for g in range(NG) if g % 2 == 1]
        N_W1 = NF - 1

        block = ctx.enter_context(nc.Block())

        @block.sync
        def _(sp):
            sp.dma_start(ids_sb[:], ids).then_inc(ids_in, 16)
            sp.dma_start(dense_sb[QUAD * DENSE_Q:QUAD * DENSE_Q + NDENSE, :], dense_t).then_inc(dense_in, 16)
            sp.dma_start(b1_sb[:], b1).then_inc(small_in, 16)
            sp.dma_start(b2_sb[:], b2).then_inc(small_in, 16)
            sp.dma_start(w2_sb[:], w2.rearrange("(t p) n -> p t n", p=P)).then_inc(weights_in, 16)
            sp.dma_start(w3_sb[:], w3).then_inc(weights_in, 16)
            sp.wait_ge(w1_cleared, 1)
            for q in range(SQ):
                for jj, j in enumerate(COLS[q]):
                    first = j * (j - 1) // 2
                    sp.dma_start(w1_sb[QUAD * q:QUAD * q + j, jj, :], w1[first:first + j, :]).then_inc(weights_in, 16)
            sp.dma_start(w1_sb[QUAD * DENSE_Q:QUAD * DENSE_Q + NDENSE, DENSE_JJ, :],
                         w1[NPAIR:NPAIR + NDENSE, :]).then_inc(weights_in, 16)
            sp.wait_ge(y_copied, CHUNKS)
            sp.dma_start(out.rearrange("(a b) o -> a (b o)", a=1), y_sb[:]).then_inc(y_out, 16)
            sp.wait_ge(y_out, 16)

        @block.gpsimd
        def _(pool):
            nc.gpsimd.memset(ident[:], 0.0).then_inc(ident_zero, 1)
            pool.wait_ge(ident_zero, 1)
            nc.gpsimd.affine_select(out=ident[:], in_=ident[:], compare_op=ALU.not_equal, fill=1.0, base=0,
                                    pattern=[[-1, P]], channel_multiplier=1).then_inc(ident_ready, 1)

            pool.wait_ge(ids_in, 16)
            for c in range(CHUNKS):
                for g in range(NG):
                    if c > 0:
                        pool.wait_ge(turned, NG * (c - 1) + g + 1)
                    for f in GROUP[g]:
                        column = ids_sb[:, c * NF + f:c * NF + f + 1]
                        nc.gpsimd.indirect_dma_start(
                            out=rows[:, f, :], out_offset=None, in_=tables[f][:, :],
                            in_offset=bass.IndirectOffsetOnAxis(ap=column, axis=0)).then_inc(gathered[g], 16)

        @block.tensor
        def _(pe):
            pe.wait_ge(ident_ready, 1)
            with pe.Fori(0, CHUNKS) as c:
                for g in range(NG):
                    pe.wait_ge(gathered[g], 16 * len(GROUP[g]) * (c + 1))
                    if g % 2 == 0:
                        pe.wait_ge(dve_rows_t, len(DVE_G) * c + g // 2)
                    else:
                        pe.wait_ge(act_rows_t, len(ACT_G) * c + g // 2)
                    for k, f in enumerate(GROUP[g]):
                        last = nc.tensor.transpose(turned_ps[g % 2][:, k, :], rows[:, f, :], ident[:])
                    last.then_inc(turned, 1)
                pe.wait_ge(dve_rows_t, len(DVE_G) * (c + 1))
                pe.wait_ge(act_rows_t, len(ACT_G) * (c + 1))
                pe.wait_ge(pads_ready, 1)
                four = rows_t[:].rearrange("d (m s) f -> d m s f", s=SQ)
                for f in range(FILLS):
                    pe.wait_ge(dve_pairs, FILLS * c + max(f - 1, 0))
                    pe.wait_ge(act_pairs, FILLS * c + max(f - 1, 0))
                    for k in range(FILLG):
                        m = f * FILLG + k
                        last = nc.tensor.matmul(
                            prod_ps[f % 2][:, k, 0:SQ * NF].rearrange("p (s f) -> p s f", s=SQ),
                            four[:, m, :, :].rearrange("d s f -> d (s f)"), four[:, m, :, 0:NF], start=True, stop=True)
                    last.then_inc(products, 1)
                pe.wait_ge(dve_pairs, FILLS * (c + 1))
                pe.wait_ge(act_pairs, FILLS * (c + 1))
                pe.wait_ge(dense_placed, c + 1)
                pe.wait_ge(weights_in, 16 * (N_W1 + 3))
                pe.wait_ge(dve_h1, c)
                pe.wait_ge(act_h1, c)
                pe.wait_ge(act_h2, c)
                pe.wait_ge(y_copied, c)
                for t in range(T1):
                    for jj in range(JJ):
                        k = USED[jj]
                        last = nc.tensor.matmul(h1_ps(t), w1_sb[0:k, jj, t * P:(t + 1) * P],
                                                pairs[0:k, jj, :], start=(jj == 0), stop=(jj == JJ - 1))
                    if t % HALF == HALF - 1:
                        last.then_inc(layer1, 1)
                pe.wait_ge(dve_h1, c + 1)
                pe.wait_ge(act_h1, c + 1)
                for u in range(T2):
                    for t in range(T1):
                        last = nc.tensor.matmul(h2_ps(u), w2_sb[:, t, u * P:(u + 1) * P], h1_sb[:, t, :],
                                                start=(t == 0), stop=(t == T1 - 1))
                    last.then_inc(layer2, 1)
                pe.wait_ge(dve_h2, c + 1)
                pe.wait_ge(act_h2, c + 1)
                for u in range(T2):
                    last = nc.tensor.matmul(y_ps, w3_sb[:, u:u + 1], h2_sb[:, u, :],
                                            start=(u == 0), stop=(u == T2 - 1))
                last.then_inc(layer3, 1)

        def turned_src(g):
            return turned_ps[g % 2][:, 0:len(GROUP[g]), :].rearrange("d f b -> d b f")

        def rows_t_dst(g):
            return rows_t[:, :, g * TG:g * TG + len(GROUP[g])]

        def pair_block(f, s, q):
            n, j = len(COLS[q]), COLS[q][0]
            src = prod_ps[f % 2][QUAD * s:QUAD * (s + 1), :, s * NF + j:s * NF + j + n].rearrange("p m j -> p j m")
            dst = pairs[QUAD * q:QUAD * (q + 1), 0:n, s * NQ + f * FILLG:s * NQ + (f + 1) * FILLG]
            return dst, src

        @block.vector
        def _(dve):
            nc.vector.memset(w1_sb[:], 0.0).then_inc(w1_cleared, 1)
            nc.vector.memset(rows_t[:, :, NF:QUAD], 0.0)
            nc.vector.memset(pairs[QUAD * DENSE_Q:P, DENSE_JJ, :], 0.0).then_inc(pads_ready, 1)
            dve.wait_ge(small_in, 32)
            with dve.Fori(0, CHUNKS) as c:
                dve.wait_ge(products, FILLS * c)
                for g in DVE_G:
                    dve.wait_ge(turned, NG * c + g + 1)
                    nc.vector.tensor_copy(rows_t_dst(g), turned_src(g)).then_inc(dve_rows_t, 1)
                dve.wait_ge(layer1, 2 * c)
                for f in range(FILLS):
                    dve.wait_ge(products, FILLS * c + f + 1)
                    for s in (0, 1):
                        for q in range(SQ):
                            last = nc.vector.tensor_copy(*pair_block(f, s, q))
                    last.then_inc(dve_pairs, 1)
                dve.wait_ge(layer2, T2 * c)
                dve.wait_ge(layer1, 2 * c + 1)
                for t in range(HALF):
                    last = nc.vector.tensor_scalar(h1_sb[:, t, :], h1_ps(t), b1_sb[:, t:t + 1], 0.0,
                                                   ALU.add, ALU.max)
                last.then_inc(dve_h1, 1)
                dve.wait_ge(layer3, c)
                dve.wait_ge(layer2, T2 * c + 1)
                nc.vector.tensor_scalar(h2_sb[:, 0, :], h2_ps(0), b2_sb[:, 0:1], 0.0,
                                        ALU.add, ALU.max).then_inc(dve_h2, 1)
                dve.wait_ge(layer3, c + 1)
                nc.vector.tensor_copy(y_sb[:, bass.ds(c * P, P)], y_ps).then_inc(y_copied, 1)

        @block.scalar
        def _(act):
            act.wait_ge(small_in, 32)
            act.wait_ge(dense_in, 16)
            act.wait_ge(pads_ready, 1)
            with act.Fori(0, CHUNKS) as c:
                act.wait_ge(products, FILLS * c)
                for g in ACT_G:
                    act.wait_ge(turned, NG * c + g + 1)
                    nc.scalar.copy(rows_t_dst(g), turned_src(g)).then_inc(act_rows_t, 1)
                act.wait_ge(layer1, 2 * c)
                dense_rows = slice(QUAD * DENSE_Q, QUAD * DENSE_Q + NDENSE)
                nc.scalar.copy(pairs[dense_rows, DENSE_JJ, :],
                               dense_sb[dense_rows, bass.ds(c * P, P)]).then_inc(dense_placed, 1)
                for f in range(FILLS):
                    act.wait_ge(products, FILLS * c + f + 1)
                    for s in (2, 3):
                        for q in range(SQ):
                            last = nc.scalar.copy(*pair_block(f, s, q))
                    last.then_inc(act_pairs, 1)
                act.wait_ge(layer2, T2 * c)
                act.wait_ge(layer1, 2 * c + 2)
                for t in range(HALF, T1):
                    last = nc.scalar.activation(h1_sb[:, t, :], h1_ps(t), ACT.Relu, bias=b1_sb[:, t:t + 1])
                last.then_inc(act_h1, 1)
                act.wait_ge(layer3, c)
                act.wait_ge(layer2, T2 * c + 2)
                nc.scalar.activation(h2_sb[:, 1, :], h2_ps(1), ACT.Relu,
                                     bias=b2_sb[:, 1:2]).then_inc(act_h2, 1)


def kernel(**inputs):
    import numpy as np
    import concourse.bacc as bacc
    from concourse.bass_utils import run_bass_kernel_spmd

    a = {k: np.asarray(v) for k, v in inputs.items()}
    n_tables = sum(k.startswith("tbl_") for k in a)
    B, NF = a["ids"].shape
    arrays = {
        "dense_t": np.ascontiguousarray(a["dense_ctx"].T),
        "ids": np.ascontiguousarray(a["ids"].reshape(B // P, P // QUAD, QUAD, NF).transpose(2, 1, 0, 3).reshape(P, -1)),
        "w1": a["W_top1"], "w2": a["W_top2"],
        "w3": np.ascontiguousarray(a["W_top3"].reshape(-1, P).T),
        "b1": np.ascontiguousarray(a["b_top1"].reshape(-1, P).T),
        "b2": np.ascontiguousarray(a["b_top2"].reshape(-1, P).T),
        **{f"tbl_{i}": a[f"tbl_{i}"] for i in range(n_tables)},
    }
    nc = bacc.Bacc("TRN2", target_bir_lowering=False, num_devices=1)
    ap = {k: nc.dram_tensor(f"in_{k}", v.shape, mybir.dt.from_np(v.dtype), kind="ExternalInput").ap()
          for k, v in arrays.items()}
    out = nc.dram_tensor("out_y", (B, 1), mybir.dt.float32, kind="ExternalOutput").ap()
    dlrm_tower_kernel(nc, ap["dense_t"], ap["ids"], [ap[f"tbl_{i}"] for i in range(n_tables)],
                      ap["w1"], ap["b1"], ap["w2"], ap["b2"], ap["w3"], out)
    r = run_bass_kernel_spmd(nc, [{f"in_{k}": v for k, v in arrays.items()}], core_ids=[0])
    return r.results[0]["out_y"]
```

```python
from contextlib import ExitStack

import concourse.bass as bass
from concourse import mybir

P = 128
QUAD = 32
WHOLE = 7
STEP_GATHERS = {"whole": 4.4, "group": 0.42, "fill": 0.84, "tiles": 0.32, "layer1": 2.5, "layer2": 1.7,
                "layer3": 0.42}
FIRST_STEP = 5.5
LANDING = 1.8


def slot_order(row_counts):
    small = sorted(range(len(row_counts)), key=lambda f: (row_counts[f], f))[:WHOLE]
    return [f for f in range(len(row_counts)) if f not in small] + sorted(small)


def pair_places(n_slots, at):
    places = []
    for j in range(1, n_slots, 2):
        places.append((j, at, j + 1))
        at += 2 * (j + 1)
    return places, at


def dlrm_tower_kernel(nc, dense, ids, ids_whole, tables, w1, b1, w2, b2, w3, out):
    F32, F32R, I32 = mybir.dt.float32, mybir.dt.float32r, mybir.dt.int32
    ALU, ACT = mybir.AluOpType, mybir.ActivationFunctionType

    NF = len(tables)
    NG = NF - WHOLE
    B, NDENSE = dense.shape
    H1, H2 = w2.shape
    CHUNKS = B // P
    T1, T2 = H1 // P, H2 // P
    SQ = P // QUAD
    NQ = P // SQ

    TG = 4
    GROUPS = NG // TG
    ROWBUFS = 2
    TABLEBUFS = 3
    FILLG = 4
    FILLS = NQ // FILLG

    TROWS = tables[NG].shape[0]
    BLOCKS = -(-TROWS // P)
    TP = TROWS // BLOCKS
    assert NG % TG == 0 and all(t.shape[0] == TROWS for t in tables[NG:]) and TP * BLOCKS == TROWS

    PLACES, NPACKED = pair_places(NF, NDENSE)
    KT = -(-NPACKED // P)
    KSIZE = [min(P, NPACKED - k * P) for k in range(KT)]
    HALF = T1 // 2
    assert HALF == T2 == 2 and NF <= QUAD and NF % 2 == 1

    ACT_BLOCKS = 2
    DVE_BLOCKS = BLOCKS - ACT_BLOCKS

    plan, turns, clock = [], [], [FIRST_STEP]

    def add(step, x):
        if step in ("whole", "group"):
            plan.append(("turn", len(turns)))
            turns.append((step, x))
        else:
            plan.append((step, x))
        clock[0] += STEP_GATHERS[step]

    def add_groups(needed=0):
        n = sum(kind == "group" for kind, _ in turns)
        while n < CHUNKS * GROUPS and (n < needed or clock[0] >= LANDING + TG * (n + 1)):
            clock[0] = max(clock[0], LANDING + TG * (n + 1))
            add("group", n)
            n += 1

    for k in range(WHOLE):
        add("whole", k)
        add_groups()
    for c in range(CHUNKS):
        add_groups(GROUPS * (c + 1))
        after = {1: ["tiles"], 3: ["layer1"], 5: ["layer2"], FILLS - 1: ["layer3"]}
        if c == CHUNKS - 1:
            after = {3: ["tiles"]}
        for f in range(FILLS):
            add("fill", (c, f))
            if c > 0:
                for step in after.get(f, []):
                    add(step, c - 1)
            add_groups()
    for step, c in (("layer1", CHUNKS - 2), ("tiles", CHUNKS - 1), ("layer2", CHUNKS - 2), ("layer1", CHUNKS - 1),
                    ("layer3", CHUNKS - 2), ("layer2", CHUNKS - 1), ("layer3", CHUNKS - 1)):
        add(step, c)
    turn_at = {t: n for n, t in enumerate(turns)}

    fills = [(step, x) for step, x in plan if step in ("fill", "tiles")]
    fill_at = {t: n for n, t in enumerate(fills)}

    with ExitStack() as ctx:
        def sb(name, shape, dt=F32):
            return ctx.enter_context(nc.sbuf_tensor(name, shape, dt))

        def psum(name, shape):
            return ctx.enter_context(nc.psum_tensor(name, shape, F32))

        def sem(name):
            return ctx.enter_context(nc.semaphore(name))

        ids_sb = sb("ids_sb", [P, CHUNKS * NG], I32)
        ident = sb("ident", [P, P])
        rows = sb("rows", [P, ROWBUFS, NG, P])
        rows_t = sb("rows_t", [P, CHUNKS, P, QUAD])
        ids_wide = sb("ids_wide", [TP, TABLEBUFS, B], I32)
        row_no = sb("row_no", [TP, BLOCKS])
        minus_row_no = sb("minus_row_no", [TP, BLOCKS])
        distance = sb("distance", [TP, ACT_BLOCKS, B])
        table_sb = sb("table_sb", [TP, TABLEBUFS, BLOCKS * P])
        table_hi = sb("table_hi", [TP, 2, BLOCKS * P], F32R)
        table_lo = sb("table_lo", [TP, 2, BLOCKS * P], F32R)
        onehot = sb("onehot", [TP, 2, BLOCKS, B], F32R)
        prods = sb("prods", [P, NF, NQ])
        packed = sb("packed", [P, CHUNKS, NPACKED])
        packed_t = sb("packed_t", [P, KT, P])
        w1_sb = sb("w1_sb", [P, KT, H1])
        w2_sb = sb("w2_sb", [P, T1, H2])
        w3_sb = sb("w3_sb", [P, T2])
        b1_sb = sb("b1_sb", [P, T1])
        b2_sb = sb("b2_sb", [P, T2])
        h1_sb = sb("h1_sb", [P, T1, P])
        h2_sb = sb("h2_sb", [P, T2, P])
        y_sb = sb("y_sb", [1, B])

        turned_ps = [psum(f"turned_ps{i}", [P, TG, P]) for i in range(2)]
        ids_ps = [psum(f"ids_ps{i}", [P, B]) for i in range(2)]
        flip_ps = [ids_ps[i][:].rearrange("p (j i) -> p j i", i=QUAD) for i in range(2)]
        SPLIT_J = 1 + B // QUAD
        DVE_PLACES = [x for x in PLACES if x[0] < SPLIT_J]
        ACT_PLACES = [x for x in PLACES if x[0] >= SPLIT_J]
        prod_ps = [psum(f"prod_ps{i}", [P, FILLG, P]) for i in range(2)]
        mlp_ps = [psum("mlp_ps_dve", [P, 4, P]), psum("mlp_ps_act", [P, 4, P])]


        def mlp_bank(c, i):
            return turned_ps[i] if c == CHUNKS - 1 else mlp_ps[i]

        def h1_ps(c, t):
            return mlp_bank(c, t // HALF)[:, t % HALF, :]

        def h2_ps(c, u):
            return mlp_bank(c, u)[:, HALF, :]

        def y_ps(c):
            return mlp_bank(c, 0)[0:1, HALF + 1, :]

        ids_in = sem("ids_in")
        ids_wide_in = [sem(f"ids_wide_in{k}") for k in range(WHOLE)]
        table_in = [sem(f"table_in{k}") for k in range(WHOLE)]
        layer_in = sem("layer_in")
        ident_zero = sem("ident_zero")
        ident_ready = sem("ident_ready")
        row_no_ready = sem("row_no_ready")
        minus_row_no_ready = sem("minus_row_no_ready")
        pads_ready = sem("pads_ready")
        gathered = [[sem(f"gathered{b}_{g}") for g in range(GROUPS)] for b in range(ROWBUFS)]
        ids_placed = sem("ids_placed")
        hi_made = sem("hi_made")
        lo_made = sem("lo_made")
        distance_made = sem("distance_made")
        dve_onehot = sem("dve_onehot")
        act_onehot = sem("act_onehot")
        onehot_used = sem("onehot_used")
        turned = sem("turned")
        turn_copied = sem("turn_copied")
        filled = sem("filled")
        dve_fill = sem("dve_fill")
        act_fill = sem("act_fill")
        flipped = sem("flipped")
        dve_packed = sem("dve_packed")
        act_packed = sem("act_packed")
        tiles_copied = sem("tiles_copied")
        layer1 = sem("layer1")
        dve_h1 = sem("dve_h1")
        act_h1 = sem("act_h1")
        layer2 = sem("layer2")
        dve_h2 = sem("dve_h2")
        act_h2 = sem("act_h2")
        layer3 = sem("layer3")
        y_copied = sem("y_copied")
        y_out = sem("y_out")
        LAYER_IN = 16 * 6

        def wait(eng, semaphore, value):
            if value > 0:
                eng.wait_ge(semaphore, value)

        def bank(step, x):
            return prod_ps[fill_at[step, x] % 2]

        def bank_free(eng, step, x):
            n = fill_at[step, x] - 2
            if n >= 0:
                before, y = fills[n]
                if before == "tiles":
                    eng.wait_ge(tiles_copied, y + 1)
                else:
                    eng.wait_ge(dve_fill, FILLS * y[0] + y[1] + 1)
                    eng.wait_ge(act_fill, FILLS * y[0] + y[1] + 1)

        block = ctx.enter_context(nc.Block())

        @block.sync
        def _(sp):
            sp.dma_start(ids_sb[:], ids).then_inc(ids_in, 16)
            for k in range(WHOLE):
                if k >= TABLEBUFS:
                    sp.wait_ge(lo_made, k - TABLEBUFS + 1)
                    sp.wait_ge(ids_placed, k - TABLEBUFS + 1)
                    sp.wait_ge(distance_made, ACT_BLOCKS * (k - TABLEBUFS + 1))
                sp.dma_start(ids_wide[:, k % TABLEBUFS, :],
                             ids_whole[k:k + 1, :].to_broadcast([TP, B])).then_inc(ids_wide_in[k], 16)
                sp.dma_start(table_sb[:, k % TABLEBUFS, :],
                             tables[NG + k].rearrange("(p b) d -> p (b d)", b=BLOCKS)).then_inc(table_in[k], 16)
                if k == 2:
                    sp.dma_start(w1_sb[:], w1.rearrange("(k p) n -> p k n", p=P)).then_inc(layer_in, 16)
                    sp.dma_start(w2_sb[:], w2.rearrange("(t p) n -> p t n", p=P)).then_inc(layer_in, 16)
                    sp.dma_start(w3_sb[:], w3).then_inc(layer_in, 16)
                    sp.dma_start(b1_sb[:], b1).then_inc(layer_in, 16)
                    sp.dma_start(b2_sb[:], b2).then_inc(layer_in, 16)
                    sp.dma_start(packed[:, :, 0:NDENSE],
                                 dense.rearrange("(c p) k -> p c k", p=P)).then_inc(layer_in, 16)
            sp.wait_ge(y_copied, CHUNKS)
            sp.dma_start(out.rearrange("(a b) o -> a (b o)", a=1), y_sb[:]).then_inc(y_out, 16)
            sp.wait_ge(y_out, 16)

        @block.gpsimd
        def _(pool):
            nc.gpsimd.iota(row_no[:], pattern=[[1, BLOCKS]], base=0, channel_multiplier=BLOCKS,
                           allow_small_or_imprecise_dtypes=True).then_inc(row_no_ready, 1)
            nc.gpsimd.memset(ident[:], 0.0).then_inc(ident_zero, 1)
            pool.wait_ge(ident_zero, 1)
            nc.gpsimd.affine_select(out=ident[:], in_=ident[:], compare_op=ALU.not_equal, fill=1.0, base=0,
                                    pattern=[[-1, P]], channel_multiplier=1).then_inc(ident_ready, 1)
            pool.wait_ge(ids_in, 16)
            for c in range(CHUNKS):
                for g in range(GROUPS):
                    if c >= ROWBUFS:
                        pool.wait_ge(turned, GROUPS * (c - ROWBUFS) + g + 1)
                    for slot in range(TG * g, TG * g + TG):
                        column = ids_sb[:, c * NG + slot:c * NG + slot + 1]
                        nc.gpsimd.indirect_dma_start(
                            out=rows[:, c % ROWBUFS, slot, :], out_offset=None, in_=tables[slot][:, :],
                            in_offset=bass.IndirectOffsetOnAxis(ap=column, axis=0)
                        ).then_inc(gathered[c % ROWBUFS][g], 16)

        @block.tensor
        def _(pe):
            def turn(n):
                if n >= 2:
                    pe.wait_ge(turn_copied, n - 1)
                kind, which = turns[n]
                if kind == "whole":
                    pe.wait_ge(hi_made, which + 1)
                    pe.wait_ge(lo_made, which + 1)
                    for b in range(BLOCKS):
                        if b < DVE_BLOCKS:
                            pe.wait_ge(dve_onehot, DVE_BLOCKS * which + b + 1)
                        else:
                            pe.wait_ge(act_onehot, ACT_BLOCKS * which + b - DVE_BLOCKS + 1)
                        for part in (table_hi, table_lo):
                            last = nc.tensor.matmul(
                                turned_ps[n % 2][:].rearrange("d a b -> d (a b)"),
                                part[:, which % 2, b * P:(b + 1) * P], onehot[:, which % 2, b, :],
                                start=(b == 0 and part is table_hi), stop=(b == BLOCKS - 1 and part is table_lo))
                        last.then_inc(onehot_used, 1)
                else:
                    c, g = divmod(which, GROUPS)
                    pe.wait_ge(gathered[c % ROWBUFS][g], 16 * TG * (c // ROWBUFS + 1))
                    for k in range(TG):
                        last = nc.tensor.transpose(turned_ps[n % 2][:, k, :],
                                                   rows[:, c % ROWBUFS, TG * g + k, :], ident[:])
                    last.then_inc(turned, 1)

            def fill(x):
                c, f = x
                if f == 0:
                    pe.wait_ge(turn_copied, 1 + max([turn_at["whole", WHOLE - 1]] + [
                        turn_at["group", GROUPS * c + g] for g in range(GROUPS)]))
                bank_free(pe, "fill", x)
                for k in range(FILLG):
                    m = FILLG * f + k
                    four = rows_t[:, c, SQ * m:SQ * (m + 1), :].rearrange("d s f -> d (s f)")
                    last = nc.tensor.matmul(bank("fill", x)[:, k, :], four, four, start=True, stop=True)
                last.then_inc(filled, 1)

            def tiles(c):
                bank_free(pe, "tiles", c)
                pe.wait_ge(dve_packed, c + 1)
                pe.wait_ge(act_packed, c + 1)
                if c == 0:
                    pe.wait_ge(layer_in, LAYER_IN)
                for k in range(KT):
                    last = nc.tensor.transpose(bank("tiles", c)[0:KSIZE[k], k, :],
                                               packed[:, c, k * P:k * P + KSIZE[k]], ident[:])
                last.then_inc(filled, 1)

            def layer1_(c):
                if c < CHUNKS - 1:
                    wait(pe, act_h2, c)
                    wait(pe, y_copied, c)
                else:
                    pe.wait_ge(turn_copied, len(turns))
                pe.wait_ge(tiles_copied, c + 1)
                for t in range(T1):
                    for k in range(KT):
                        last = nc.tensor.matmul(h1_ps(c, t), w1_sb[0:KSIZE[k], k, t * P:(t + 1) * P],
                                                packed_t[0:KSIZE[k], k, :], start=(k == 0), stop=(k == KT - 1))
                    if t % HALF == HALF - 1:
                        last.then_inc(layer1, 1)

            def layer2_(c):
                pe.wait_ge(dve_h1, c + 1)
                pe.wait_ge(act_h1, c + 1)
                for u in range(T2):
                    for t in range(T1):
                        last = nc.tensor.matmul(h2_ps(c, u), w2_sb[:, t, u * P:(u + 1) * P], h1_sb[:, t, :],
                                                start=(t == 0), stop=(t == T1 - 1))
                    last.then_inc(layer2, 1)

            def layer3_(c):
                pe.wait_ge(dve_h2, c + 1)
                pe.wait_ge(act_h2, c + 1)
                for u in range(T2):
                    last = nc.tensor.matmul(y_ps(c), w3_sb[:, u:u + 1], h2_sb[:, u, :],
                                            start=(u == 0), stop=(u == T2 - 1))
                last.then_inc(layer3, 1)

            pe.wait_ge(ident_ready, 1)
            pe.wait_ge(pads_ready, 1)
            steps = {"turn": turn, "fill": fill, "tiles": tiles,
                     "layer1": layer1_, "layer2": layer2_, "layer3": layer3_}
            for step, x in plan:
                steps[step](x)

        def copy_block(copy, x, s):
            part = slice(QUAD * s, QUAD * (s + 1))
            f = x[1]
            return copy(prods[part, 1:NF, f * FILLG:(f + 1) * FILLG].rearrange("p j m -> p m j"),
                        bank("fill", x)[part, :, QUAD * s + 1:QUAD * s + NF])

        @block.vector
        def _(dve):
            def fill(x):
                c, f = x
                if f == 0:
                    wait(dve, flipped, 2 * c)
                dve.wait_ge(filled, fill_at["fill", x] + 1)
                for s in (0, 1):
                    last = copy_block(nc.vector.tensor_copy, x, s)
                last.then_inc(dve_fill, 1)
                if f == FILLS - 1:
                    pack(c)

            def pack(c):
                dve.wait_ge(dve_fill, FILLS * (c + 1))
                dve.wait_ge(act_fill, FILLS * (c + 1))
                wait(dve, act_packed, c)
                wait(dve, dve_packed, c)
                for i, first, end in ((1, SPLIT_J, NF), (0, 1, SPLIT_J)):
                    nc.vector.transpose(ids_ps[i][:, 0:QUAD * (end - first)],
                                        prods[:, first:end, :].rearrange("p j m -> p (j m)")).then_inc(flipped, 1)
                dve.wait_ge(flipped, 2 * c + 2)
                for j, at, width in DVE_PLACES:
                    last = nc.vector.tensor_copy(packed[:, c, at:at + 2 * width].rearrange("p (a i) -> p a i", a=2),
                                                 flip_ps[0][:, j - 1:j + 1, 0:width])
                last.then_inc(dve_packed, 1)

            def layer1_(c):
                wait(dve, layer2, 2 * c)
                dve.wait_ge(layer1, 2 * c + 1)
                for t in range(HALF):
                    last = nc.vector.tensor_scalar(h1_sb[:, t, :], h1_ps(c, t), b1_sb[:, t:t + 1], 0.0,
                                                   ALU.add, ALU.max)
                last.then_inc(dve_h1, 1)

            def layer2_(c):
                wait(dve, layer3, c)
                dve.wait_ge(layer2, T2 * c + 1)
                nc.vector.tensor_scalar(h2_sb[:, 0, :], h2_ps(c, 0), b2_sb[:, 0:1], 0.0,
                                        ALU.add, ALU.max).then_inc(dve_h2, 1)

            def layer3_(c):
                dve.wait_ge(layer3, c + 1)
                nc.vector.tensor_copy(y_sb[:, c * P:(c + 1) * P], y_ps(c)).then_inc(y_copied, 1)

            nc.vector.memset(rows_t[:, :, :, NF:QUAD].rearrange("d c b f -> d (c b) f"), 0.0).then_inc(pads_ready, 1)
            dve.wait_ge(row_no_ready, 1)
            for k in range(WHOLE):
                dve.wait_ge(hi_made, k + 1)
                dve.wait_ge(table_in[k], 16)
                wait(dve, onehot_used, BLOCKS * (k - 1))
                nc.vector.tensor_tensor(table_lo[:, k % 2, :], table_sb[:, k % TABLEBUFS, :],
                                        table_hi[:, k % 2, :].bitcast(F32), ALU.subtract).then_inc(lo_made, 1)
                dve.wait_ge(ids_placed, k + 1)
                for b in range(DVE_BLOCKS):
                    nc.vector.tensor_scalar(onehot[:, k % 2, b, :], ids_ps[k % 2][0:TP, :], row_no[:, b:b + 1], None,
                                            ALU.is_equal).then_inc(dve_onehot, 1)
            dve.wait_ge(layer_in, LAYER_IN)
            steps = {"fill": fill, "layer1": layer1_, "layer2": layer2_, "layer3": layer3_}
            for step, x in plan:
                if step in steps:
                    steps[step](x)

        @block.scalar
        def _(act):
            def turn(n):
                kind, which = turns[n]
                if kind == "whole":
                    if which + 1 < WHOLE:
                        split(which + 1)
                        onehots(which + 1)
                    act.wait_ge(onehot_used, BLOCKS * (which + 1))
                    nc.scalar.copy(rows_t[:, :, :, NG + which].rearrange("d c b -> d (c b)"),
                                   turned_ps[n % 2][:].rearrange("d a b -> d (a b)")).then_inc(turn_copied, 1)
                else:
                    c, g = divmod(which, GROUPS)
                    act.wait_ge(turned, which + 1)
                    nc.scalar.copy(rows_t[:, c, :, TG * g:TG * g + TG],
                                   turned_ps[n % 2][:].rearrange("d f b -> d b f")).then_inc(turn_copied, 1)

            def split(k):
                act.wait_ge(ids_wide_in[k], 16)
                wait(act, dve_onehot, DVE_BLOCKS * (k - 1))
                nc.scalar.copy(ids_ps[k % 2][0:TP, :], ids_wide[:, k % TABLEBUFS, :]).then_inc(ids_placed, 1)
                act.wait_ge(table_in[k], 16)
                wait(act, onehot_used, BLOCKS * (k - 1))
                nc.scalar.copy(table_hi[:, k % 2, :], table_sb[:, k % TABLEBUFS, :]).then_inc(hi_made, 1)

            def onehots(k):
                wait(act, act_onehot, ACT_BLOCKS * k)
                for i in range(ACT_BLOCKS):
                    b = DVE_BLOCKS + i
                    nc.scalar.activation(distance[:, i, :], ids_wide[:, k % TABLEBUFS, :], ACT.Abs,
                                         bias=minus_row_no[:, b:b + 1]).then_inc(distance_made, 1)
                for i in range(ACT_BLOCKS):
                    act.wait_ge(distance_made, ACT_BLOCKS * k + i + 1)
                    nc.scalar.activation(onehot[:, k % 2, DVE_BLOCKS + i, :], distance[:, i, :], ACT.Relu,
                                         bias=1.0, scale=-1.0).then_inc(act_onehot, 1)

            def fill(x):
                c, f = x
                if f == 0:
                    wait(act, flipped, 2 * c)
                act.wait_ge(filled, fill_at["fill", x] + 1)
                for s in (2, 3):
                    last = copy_block(nc.scalar.copy, x, s)
                last.then_inc(act_fill, 1)
                if f == FILLS - 1:
                    act.wait_ge(flipped, 2 * c + 1)
                    for j, at, width in ACT_PLACES:
                        last = nc.scalar.copy(packed[:, c, at:at + 2 * width].rearrange("p (a i) -> p a i", a=2),
                                              flip_ps[1][:, j - SPLIT_J:j - SPLIT_J + 2, 0:width])
                    last.then_inc(act_packed, 1)

            def tiles(c):
                wait(act, layer1, 2 * c)
                act.wait_ge(filled, fill_at["tiles", c] + 1)
                for k in range(KT):
                    last = nc.scalar.copy(packed_t[0:KSIZE[k], k, :], bank("tiles", c)[0:KSIZE[k], k, :])
                last.then_inc(tiles_copied, 1)

            def layer1_(c):
                wait(act, layer2, 2 * c)
                act.wait_ge(layer1, 2 * c + 2)
                for t in range(HALF, T1):
                    last = nc.scalar.activation(h1_sb[:, t, :], h1_ps(c, t), ACT.Relu, bias=b1_sb[:, t:t + 1])
                last.then_inc(act_h1, 1)

            def layer2_(c):
                wait(act, layer3, c)
                act.wait_ge(layer2, T2 * c + 2)
                nc.scalar.activation(h2_sb[:, 1, :], h2_ps(c, 1), ACT.Relu, bias=b2_sb[:, 1:2]).then_inc(act_h2, 1)

            act.wait_ge(row_no_ready, 1)
            nc.scalar.activation(minus_row_no[:], row_no[:], ACT.Identity, scale=-1.0).then_inc(minus_row_no_ready, 1)
            act.wait_ge(minus_row_no_ready, 1)
            split(0)
            onehots(0)
            steps = {"turn": turn, "fill": fill, "tiles": tiles, "layer1": layer1_, "layer2": layer2_}
            for n, (step, x) in enumerate(plan):
                if step == "fill" and x == (0, 0):
                    act.wait_ge(layer_in, LAYER_IN)
                if step in steps:
                    steps[step](x)


def kernel(**inputs):
    import numpy as np
    import concourse.bacc as bacc
    from concourse.bass_utils import run_bass_kernel_spmd

    a = {k: np.asarray(v) for k, v in inputs.items()}
    B, NF = a["ids"].shape
    order = slot_order([a[f"tbl_{f}"].shape[0] for f in range(NF)])
    NG = NF - WHOLE
    ids = a["ids"][:, order].reshape(B // P, P // QUAD, QUAD, NF).transpose(0, 2, 1, 3).reshape(B // P, P, NF)
    n_dense = a["dense_ctx"].shape[1]
    places, n_packed = pair_places(NF, n_dense)
    n_rows = a["W_top1"].shape[0]
    w1 = np.zeros((-(-n_packed // P) * P, a["W_top1"].shape[1]), a["W_top1"].dtype)
    for first, at, width in places:
        for j in (first, first + 1):
            for i in range(j):
                lo, hi = sorted((order[i], order[j]))
                w1[at + (j - first) * width + i] = a["W_top1"][hi * (hi - 1) // 2 + lo]
    w1[:n_dense] = a["W_top1"][n_rows - n_dense:]
    arrays = {
        "dense": a["dense_ctx"],
        "ids": np.ascontiguousarray(ids[:, :, :NG].transpose(1, 0, 2).reshape(P, -1)),
        "ids_whole": np.ascontiguousarray(ids[:, :, NG:].transpose(2, 0, 1).reshape(WHOLE, B)),
        "w1": w1, "w2": a["W_top2"],
        "w3": np.ascontiguousarray(a["W_top3"].reshape(-1, P).T),
        "b1": np.ascontiguousarray(a["b_top1"].reshape(-1, P).T),
        "b2": np.ascontiguousarray(a["b_top2"].reshape(-1, P).T),
        **{f"tbl_{f}": a[f"tbl_{f}"] for f in range(NF)},
    }
    nc = bacc.Bacc("TRN2", target_bir_lowering=False, num_devices=1)
    ap = {k: nc.dram_tensor(f"in_{k}", v.shape, mybir.dt.from_np(v.dtype), kind="ExternalInput").ap()
          for k, v in arrays.items()}
    out = nc.dram_tensor("out_y", (B, 1), mybir.dt.float32, kind="ExternalOutput").ap()
    dlrm_tower_kernel(nc, ap["dense"], ap["ids"], ap["ids_whole"], [ap[f"tbl_{f}"] for f in order],
                      ap["w1"], ap["b1"], ap["w2"], ap["b2"], ap["w3"], out)
    r = run_bass_kernel_spmd(nc, [{f"in_{k}": v for k, v in arrays.items()}], core_ids=[0])
    return r.results[0]["out_y"]
```

```python
from contextlib import ExitStack

import concourse.bass as bass
from concourse import mybir

P = 128
QUAD = 32
WHOLE = 12
ORDER = (
    "wwwwgwwgwwgwwgwwgwwgwwgwffwgfgwwgfwwgwpwgffffpgTg1g2ffffp3TggT1g2g3ffffp1T21323"
)
STEPS = {"w": "whole", "g": "group", "f": "fill", "p": "pack", "T": "tiles", "1": "layer1", "2": "layer2",
         "3": "layer3"}


def slot_order(row_counts):
    small = sorted(range(len(row_counts)), key=lambda f: (row_counts[f], f))[:WHOLE]
    return sorted(small) + [f for f in range(len(row_counts)) if f not in small]


def pair_places(n_slots, at):
    places = []
    for j in range(1, n_slots, 2):
        places.append((j, at, j + 1))
        at += 2 * (j + 1)
    return places, at


def dlrm_tower_kernel(nc, dense, ids, ids_whole, tables, w1, b1, w2, b2, w3, out):
    F32, F32R, I32 = mybir.dt.float32, mybir.dt.float32r, mybir.dt.int32
    ALU, ACT = mybir.AluOpType, mybir.ActivationFunctionType

    NF = len(tables)
    NG = NF - WHOLE
    B, NDENSE = dense.shape
    H1, H2 = w2.shape
    CHUNKS = B // P
    T1, T2 = H1 // P, H2 // P
    SQ = P // QUAD
    NQ = P // SQ

    TG = 4
    GROUPS = [(c, first, min(first + TG, NF)) for c in range(CHUNKS)
              for first in range(WHOLE if c else 0, NF, TG)]
    B1 = B - P
    ROWBUFS = 2
    TABLEBUFS = 5
    LAYERS_AFTER = 7
    PARTBUFS = 3
    AHEAD = PARTBUFS - 1
    FILLG = 8
    FILLS = NQ // FILLG

    TROWS = tables[0].shape[0]
    BLOCKS = -(-TROWS // P)
    TP = TROWS // BLOCKS
    assert all(t.shape[0] == TROWS for t in tables[:WHOLE]) and TP * BLOCKS == TROWS

    PLACES, NPACKED = pair_places(NF, NDENSE)
    KT = -(-NPACKED // P)
    KSIZE = [min(P, NPACKED - k * P) for k in range(KT)]
    HALF = T1 // 2
    assert HALF == T2 == 2 and NF <= QUAD and NF % 2 == 1

    ACT_BLOCKS = 2
    DVE_BLOCKS = BLOCKS - ACT_BLOCKS
    HALVES = [list(range(h * DVE_BLOCKS // 2, (h + 1) * DVE_BLOCKS // 2)) + [DVE_BLOCKS + h] for h in range(2)]
    assert ACT_BLOCKS == 2 and DVE_BLOCKS % 2 == 0

    plan = []
    for letter in ORDER:
        n = sum(step == STEPS[letter] for step, _ in plan)
        plan.append((STEPS[letter], divmod(n, 2) if letter == "w" else divmod(n, FILLS) if letter == "f" else n))
    assert [ORDER.count(x) for x in "wgfpT123"] == [2 * WHOLE, len(GROUPS), FILLS * CHUNKS] + 5 * [CHUNKS]
    turns = [(step, x[0] if step == "whole" else x) for step, x in plan
             if step == "group" or step == "whole" and x[1] == 1]

    def groups_of(c):
        return [n for n in range(len(GROUPS)) if GROUPS[n][0] == c]

    turn_at = {t: n for n, t in enumerate(turns)}

    fills = [(step, x) for step, x in plan if step in ("fill", "tiles")]
    fill_at = {t: n for n, t in enumerate(fills)}

    with ExitStack() as ctx:
        def sb(name, shape, dt=F32):
            return ctx.enter_context(nc.sbuf_tensor(name, shape, dt))

        def psum(name, shape):
            return ctx.enter_context(nc.psum_tensor(name, shape, F32))

        def sem(name):
            return ctx.enter_context(nc.semaphore(name))

        ids_sb = sb("ids_sb", [P, NF + (CHUNKS - 1) * NG], I32)
        ident = sb("ident", [P, P])
        rows = sb("rows", [P, ROWBUFS, NF, P])
        rows_t = sb("rows_t", [P, CHUNKS, P, NF])
        ids_wide = sb("ids_wide", [TP, TABLEBUFS, B1], I32)
        row_no = sb("row_no", [TP, BLOCKS])
        minus_row_no = sb("minus_row_no", [TP, BLOCKS])
        distance = sb("distance", [TP, ACT_BLOCKS, B1])
        table_sb = sb("table_sb", [TP, TABLEBUFS, BLOCKS * P])
        table_hi = sb("table_hi", [TP, PARTBUFS, BLOCKS * P], F32R)
        table_lo = sb("table_lo", [TP, PARTBUFS, BLOCKS * P], F32R)
        onehot = sb("onehot", [TP, PARTBUFS, BLOCKS, B1], F32R)
        prods = sb("prods", [P, NF, NQ])
        packed = sb("packed", [P, CHUNKS, NPACKED])
        packed_t = sb("packed_t", [P, KT, P])
        w1_sb = sb("w1_sb", [P, KT, H1])
        w2_sb = sb("w2_sb", [P, T1, H2])
        w3_sb = sb("w3_sb", [P, T2])
        b1_sb = sb("b1_sb", [P, T1])
        b2_sb = sb("b2_sb", [P, T2])
        h1_sb = sb("h1_sb", [P, T1, P])
        h2_sb = sb("h2_sb", [P, T2, P])
        y_sb = sb("y_sb", [1, B])

        turned_ps = [psum(f"turned_ps{i}", [P, TG, P]) for i in range(2)]
        flipped_ps = [psum(f"flipped_ps{i}", [P, B]) for i in range(2)]
        SPLIT_J = 11
        DVE_PLACES = [x for x in PLACES if x[0] < SPLIT_J]
        ACT_PLACES = [x for x in PLACES if x[0] >= SPLIT_J]
        prod_ps = [psum(f"prod_ps{i}", [P, 4, P]) for i in range(2)]
        mlp_ps = [psum("mlp_ps_dve", [P, 4, P]), psum("mlp_ps_act", [P, 4, P])]

        row_ps = flipped_ps[0][0:TP, 0:BLOCKS]

        def flip_ps(c, i):
            return mlp_ps[i][:].rearrange("p a b -> p (a b)") if c == 0 else flipped_ps[i][:]

        def mlp_bank(c, i):
            return turned_ps[i] if c == CHUNKS - 1 else mlp_ps[i]

        def h1_ps(c, t):
            return mlp_bank(c, t // HALF)[:, t % HALF, :]

        def h2_ps(c, u):
            return mlp_bank(c, u)[:, HALF, :]

        def y_ps(c):
            return mlp_bank(c, 0)[0:1, HALF + 1, :]

        ids_in = sem("ids_in")
        ids_wide_in = [sem(f"ids_wide_in{k}") for k in range(WHOLE)]
        table_in = [sem(f"table_in{k}") for k in range(WHOLE)]
        layer_in = sem("layer_in")
        ident_zero = sem("ident_zero")
        ident_ready = sem("ident_ready")
        row_no_ready = sem("row_no_ready")
        minus_row_no_ready = sem("minus_row_no_ready")
        prod_ps_zero = sem("prod_ps_zero")
        gathered = [sem(f"gathered_c{c}_s{first}") for c, first, _ in GROUPS]
        rows_placed = sem("rows_placed")
        hi_made = sem("hi_made")
        lo_made = sem("lo_made")
        distance_made = sem("distance_made")
        dve_onehot = sem("dve_onehot")
        act_onehot = sem("act_onehot")
        product_done = sem("product_done")
        turned = sem("turned")
        act_turned = sem("act_turned")
        dve_turned = sem("dve_turned")
        filled = sem("filled")
        dve_fill = sem("dve_fill")
        act_fill = sem("act_fill")
        flipped = sem("flipped")
        dve_packed = sem("dve_packed")
        act_packed = sem("act_packed")
        tiles_copied = sem("tiles_copied")
        layer1 = sem("layer1")
        dve_h1 = sem("dve_h1")
        act_h1 = sem("act_h1")
        layer2 = sem("layer2")
        dve_h2 = sem("dve_h2")
        act_h2 = sem("act_h2")
        layer3 = sem("layer3")
        y_copied = sem("y_copied")
        y_out = sem("y_out")
        LAYER_IN = 16 * 6

        def wait(eng, semaphore, value):
            if value > 0:
                eng.wait_ge(semaphore, value)

        def bank(step, x):
            return prod_ps[fill_at[step, x] % 2]

        def fill_bank(x):
            return bank("fill", x)[:].rearrange("p a b -> p (a b)")[:, 0:FILLG * QUAD].rearrange(
                "p (m j) -> p m j", j=QUAD)

        def dve_turns(n):
            return n > turn_at["whole", WHOLE - 1] and (len(turns) - n) % 2 == 1

        def wait_turns(eng, n):
            by_dve = sum(dve_turns(i) for i in range(n + 1))
            eng.wait_ge(act_turned, n + 1 - by_dve)
            wait(eng, dve_turned, by_dve)

        def copy_group(copy, n):
            c, first, end = GROUPS[n]
            return copy(rows_t[:, c, :, first:end],
                        turned_ps[turn_at["group", n] % 2][:, 0:end - first, :].rearrange("d f b -> d b f"))

        def bank_free(eng, step, x):
            n = fill_at[step, x] - 2
            if n >= 0:
                before, y = fills[n]
                if before == "tiles":
                    eng.wait_ge(tiles_copied, y + 1)
                else:
                    eng.wait_ge((dve_fill, act_fill)[y[1] % 2], FILLS // 2 * y[0] + y[1] // 2 + 1)

        block = ctx.enter_context(nc.Block())

        @block.sync
        def _(sp):
            sp.dma_start(ids_sb[:], ids).then_inc(ids_in, 16)
            for k in range(WHOLE):
                if k >= TABLEBUFS:
                    sp.wait_ge(lo_made, k - TABLEBUFS + 1)
                    sp.wait_ge(dve_onehot, 2 * (k - TABLEBUFS + 1))
                    sp.wait_ge(distance_made, ACT_BLOCKS * (k - TABLEBUFS + 1))
                sp.dma_start(ids_wide[:, k % TABLEBUFS, :],
                             ids_whole[k:k + 1, :].to_broadcast([TP, B1])).then_inc(ids_wide_in[k], 16)
                sp.dma_start(table_sb[:, k % TABLEBUFS, :],
                             tables[k].rearrange("(p b) d -> p (b d)", b=BLOCKS)).then_inc(table_in[k], 16)
                if k == LAYERS_AFTER:
                    sp.dma_start(w1_sb[:], w1.rearrange("(k p) n -> p k n", p=P)).then_inc(layer_in, 16)
                    sp.dma_start(w2_sb[:], w2.rearrange("(t p) n -> p t n", p=P)).then_inc(layer_in, 16)
                    sp.dma_start(w3_sb[:], w3).then_inc(layer_in, 16)
                    sp.dma_start(b1_sb[:], b1).then_inc(layer_in, 16)
                    sp.dma_start(b2_sb[:], b2).then_inc(layer_in, 16)
                    sp.dma_start(packed[:, :, 0:NDENSE],
                                 dense.rearrange("(c p) k -> p c k", p=P)).then_inc(layer_in, 16)
            sp.wait_ge(y_copied, CHUNKS)
            sp.dma_start(out.rearrange("(a b) o -> a (b o)", a=1), y_sb[:]).then_inc(y_out, 16)
            sp.wait_ge(y_out, 16)

        @block.gpsimd
        def _(pool):
            nc.gpsimd.iota(row_no[:], pattern=[[1, BLOCKS]], base=0, channel_multiplier=BLOCKS,
                           allow_small_or_imprecise_dtypes=True).then_inc(row_no_ready, 1)
            nc.gpsimd.memset(ident[:], 0.0).then_inc(ident_zero, 1)
            pool.wait_ge(ident_zero, 1)
            nc.gpsimd.affine_select(out=ident[:], in_=ident[:], compare_op=ALU.not_equal, fill=1.0, base=0,
                                    pattern=[[-1, P]], channel_multiplier=1).then_inc(ident_ready, 1)
            pool.wait_ge(ids_in, 16)
            column = 0
            for n, (c, first, end) in enumerate(GROUPS):
                if c >= ROWBUFS:
                    pool.wait_ge(turned, 1 + max(m for m, (c1, first1, _) in enumerate(GROUPS)
                                                 if c1 == c - ROWBUFS and first1 < end))
                for slot in range(first, end):
                    nc.gpsimd.indirect_dma_start(
                        out=rows[:, c % ROWBUFS, slot, :], out_offset=None, in_=tables[slot][:, :],
                        in_offset=bass.IndirectOffsetOnAxis(ap=ids_sb[:, column:column + 1], axis=0)
                    ).then_inc(gathered[n], 16)
                    column += 1

        @block.tensor
        def _(pe):
            def turn_bank(n):
                if n >= 2:
                    wait_turns(pe, n - 2)
                return turned_ps[n % 2]

            def whole(x):
                k, h = x
                ps = turn_bank(turn_at["whole", k])
                for part, made in ((table_hi, hi_made), (table_lo, lo_made)):
                    pe.wait_ge(made, k + 1)
                    for b in HALVES[h]:
                        if part is table_hi:
                            if b < DVE_BLOCKS:
                                pe.wait_ge(dve_onehot, 2 * k + h + 1)
                            else:
                                pe.wait_ge(act_onehot, k + 1)
                        last = nc.tensor.matmul(
                            ps[:].rearrange("d a b -> d (a b)")[:, 0:B1],
                            part[:, k % PARTBUFS, b * P:(b + 1) * P], onehot[:, k % PARTBUFS, b, :],
                            start=(b == HALVES[0][0] and part is table_hi),
                            stop=(b == HALVES[1][-1] and part is table_lo))
                last.then_inc(product_done, 1)

            def group(n):
                c, first, end = GROUPS[n]
                ps = turn_bank(turn_at["group", n])
                pe.wait_ge(gathered[n], 16 * (end - first))
                for slot in range(first, end):
                    last = nc.tensor.transpose(ps[:, slot - first, :], rows[:, c % ROWBUFS, slot, :], ident[:])
                last.then_inc(turned, 1)

            def fill(x):
                c, f = x
                if f == 0:
                    needed = [turn_at["group", n] for n in groups_of(c)]
                    if c > 0:
                        needed.append(turn_at["whole", WHOLE - 1])
                    wait_turns(pe, max(needed))
                bank_free(pe, "fill", x)
                for k in range(FILLG):
                    m = FILLG * f + k
                    for s in range(SQ):
                        sample = rows_t[:, c, SQ * m + s, :]
                        last = nc.tensor.matmul(fill_bank(x)[QUAD * s:QUAD * s + NF - 1, k, 1:NF],
                                                sample[:, 0:NF - 1], sample[:, 1:NF], start=True, stop=True)
                last.then_inc(filled, 1)

            def tiles(c):
                bank_free(pe, "tiles", c)
                pe.wait_ge(dve_packed, c + 1)
                pe.wait_ge(act_packed, c + 1)
                if c == 0:
                    pe.wait_ge(layer_in, LAYER_IN)
                for k in range(KT):
                    last = nc.tensor.transpose(bank("tiles", c)[0:KSIZE[k], k, :],
                                               packed[:, c, k * P:k * P + KSIZE[k]], ident[:])
                last.then_inc(filled, 1)

            def layer1_(c):
                if c < CHUNKS - 1:
                    wait(pe, act_h2, c)
                    wait(pe, y_copied, c)
                else:
                    wait_turns(pe, len(turns) - 1)
                pe.wait_ge(tiles_copied, c + 1)
                for t in range(T1):
                    for k in range(KT):
                        last = nc.tensor.matmul(h1_ps(c, t), w1_sb[0:KSIZE[k], k, t * P:(t + 1) * P],
                                                packed_t[0:KSIZE[k], k, :], start=(k == 0), stop=(k == KT - 1))
                    if t % HALF == HALF - 1:
                        last.then_inc(layer1, 1)

            def layer2_(c):
                pe.wait_ge(dve_h1, HALF * (c + 1))
                for u in range(T2):
                    for t in range(T1):
                        if u == 0 and t >= HALF:
                            pe.wait_ge(act_h1, HALF * c + t - HALF + 1)
                        last = nc.tensor.matmul(h2_ps(c, u), w2_sb[:, t, u * P:(u + 1) * P], h1_sb[:, t, :],
                                                start=(t == 0), stop=(t == T1 - 1))
                    last.then_inc(layer2, 1)

            def layer3_(c):
                pe.wait_ge(dve_h2, c + 1)
                pe.wait_ge(act_h2, c + 1)
                for u in range(T2):
                    last = nc.tensor.matmul(y_ps(c), w3_sb[:, u:u + 1], h2_sb[:, u, :],
                                            start=(u == 0), stop=(u == T2 - 1))
                last.then_inc(layer3, 1)

            pe.wait_ge(ident_ready, 1)
            pe.wait_ge(prod_ps_zero, 2)
            steps = {"whole": whole, "group": group, "fill": fill, "tiles": tiles,
                     "layer1": layer1_, "layer2": layer2_, "layer3": layer3_}
            for step, x in plan:
                if step in steps:
                    steps[step](x)

        def copy_fill(copy, x):
            samples = slice(x[1] * FILLG, (x[1] + 1) * FILLG)
            return copy(prods[:, 1:NF, samples].rearrange("p j m -> p m j"), fill_bank(x)[:, :, 1:NF])

        def copy_pairs(copy, c, i, j, at, width):
            first = QUAD * (j - (1, SPLIT_J)[i])
            return copy(packed[:, c, at:at + 2 * width].rearrange("p (a i) -> p a i", a=2),
                        flip_ps(c, i)[:, first:first + 2 * QUAD].rearrange("p (j i) -> p j i", i=QUAD)[:, :, 0:width])

        @block.vector
        def _(dve):
            def fill(x):
                c, f = x
                if f == 0:
                    wait(dve, flipped, 2 * c)
                if f % 2 == 0:
                    dve.wait_ge(filled, fill_at["fill", x] + 1)
                    copy_fill(nc.vector.tensor_copy, x).then_inc(dve_fill, 1)

            def group(n):
                if dve_turns(turn_at["group", n]):
                    dve.wait_ge(turned, n + 1)
                    copy_group(nc.vector.tensor_copy, n).then_inc(dve_turned, 1)

            def flip(c, i, first, end):
                at = QUAD * (first - (1, SPLIT_J)[i])
                nc.vector.transpose(flip_ps(c, i)[:, at:at + QUAD * (end - first)],
                                    prods[:, first:end, :].rearrange("p j m -> p (j m)")).then_inc(flipped, 1)

            def pack(c):
                dve.wait_ge(dve_fill, FILLS // 2 * (c + 1))
                dve.wait_ge(act_fill, FILLS // 2 * (c + 1))
                if c == 1:
                    dve.wait_ge(dve_onehot, 2 * WHOLE)
                elif c > 1:
                    dve.wait_ge(act_packed, c)
                    dve.wait_ge(dve_packed, c)
                flip(c, 1, SPLIT_J, NF)
                flip(c, 0, 1, SPLIT_J)
                dve.wait_ge(flipped, 2 * c + 2)
                for place in DVE_PLACES:
                    last = copy_pairs(nc.vector.tensor_copy, c, 0, *place)
                last.then_inc(dve_packed, 1)

            def layer1_(c):
                wait(dve, layer2, 2 * c)
                dve.wait_ge(layer1, 2 * c + 1)
                for t in range(HALF):
                    nc.vector.tensor_scalar(h1_sb[:, t, :], h1_ps(c, t), b1_sb[:, t:t + 1], 0.0,
                                            ALU.add, ALU.max).then_inc(dve_h1, 1)

            def layer2_(c):
                wait(dve, layer3, c)
                dve.wait_ge(layer2, T2 * c + 1)
                nc.vector.tensor_scalar(h2_sb[:, 0, :], h2_ps(c, 0), b2_sb[:, 0:1], 0.0,
                                        ALU.add, ALU.max).then_inc(dve_h2, 1)

            def layer3_(c):
                dve.wait_ge(layer3, c + 1)
                nc.vector.tensor_copy(y_sb[:, c * P:(c + 1) * P], y_ps(c)).then_inc(y_copied, 1)

            for ps in prod_ps:
                nc.vector.memset(ps[:], 0.0).then_inc(prod_ps_zero, 1)
            dve.wait_ge(row_no_ready, 1)
            nc.vector.tensor_copy(row_ps, row_no[:]).then_inc(rows_placed, 1)
            dve.wait_ge(rows_placed, 1)

            def rest(k):
                dve.wait_ge(hi_made, k + 1)
                dve.wait_ge(table_in[k], 16)
                wait(dve, product_done, 2 * (k - PARTBUFS + 1))
                nc.vector.tensor_tensor(table_lo[:, k % PARTBUFS, :], table_sb[:, k % TABLEBUFS, :],
                                        table_hi[:, k % PARTBUFS, :].bitcast(F32), ALU.subtract).then_inc(lo_made, 1)

            def onehots(k, h):
                dve.wait_ge(ids_wide_in[k], 16)
                blocks = HALVES[h][:-1]
                shape = [TP, len(blocks), B1]
                nc.vector.tensor_tensor(
                    onehot[:, k % PARTBUFS, blocks[0]:blocks[-1] + 1, :],
                    ids_wide[:, k % TABLEBUFS, :].unsqueeze(1).to_broadcast(shape),
                    row_ps[:, blocks[0]:blocks[-1] + 1].unsqueeze(2).to_broadcast(shape),
                    ALU.is_equal).then_inc(dve_onehot, 1)

            def whole(x):
                k, h = x[0] + AHEAD, x[1]
                if k < WHOLE:
                    if h == 0:
                        rest(k)
                    onehots(k, h)

            for k in range(AHEAD):
                onehots(k, 0)
                onehots(k, 1)
                rest(k)
            steps = {"whole": whole, "group": group, "fill": fill, "pack": pack,
                     "layer1": layer1_, "layer2": layer2_, "layer3": layer3_}
            for step, x in plan:
                if (step, x) == ("fill", (0, 0)):
                    dve.wait_ge(layer_in, LAYER_IN)
                if step in steps:
                    steps[step](x)

        @block.scalar
        def _(act):
            def whole(x):
                k, h = x
                if h == 0 and k + AHEAD < WHOLE:
                    split(k + AHEAD)
                    distances(k + AHEAD)
                elif k + AHEAD < WHOLE:
                    onehots(k + AHEAD)
                if h == 1:
                    act.wait_ge(product_done, 2 * (k + 1))
                    nc.scalar.copy(rows_t[:, 1:, :, k].rearrange("d c b -> d (c b)"),
                                   turned_ps[turn_at["whole", k] % 2][:].rearrange("d a b -> d (a b)")[:, 0:B1]
                                   ).then_inc(act_turned, 1)

            def group(n):
                if not dve_turns(turn_at["group", n]):
                    act.wait_ge(turned, n + 1)
                    copy_group(nc.scalar.copy, n).then_inc(act_turned, 1)

            def split(k):
                act.wait_ge(table_in[k], 16)
                wait(act, product_done, 2 * (k - PARTBUFS + 1))
                nc.scalar.copy(table_hi[:, k % PARTBUFS, :], table_sb[:, k % TABLEBUFS, :]).then_inc(hi_made, 1)

            def distances(k):
                act.wait_ge(ids_wide_in[k], 16)
                wait(act, act_onehot, k)
                for i in range(ACT_BLOCKS):
                    b = DVE_BLOCKS + i
                    nc.scalar.activation(distance[:, i, :], ids_wide[:, k % TABLEBUFS, :], ACT.Abs,
                                         bias=minus_row_no[:, b:b + 1]).then_inc(distance_made, 1)

            def onehots(k):
                act.wait_ge(distance_made, ACT_BLOCKS * (k + 1))
                nc.scalar.activation(onehot[:, k % PARTBUFS, DVE_BLOCKS:BLOCKS, :], distance[:], ACT.Relu,
                                     bias=1.0, scale=-1.0).then_inc(act_onehot, 1)

            def fill(x):
                c, f = x
                if f == 0:
                    wait(act, flipped, 2 * c)
                if f % 2 == 1:
                    act.wait_ge(filled, fill_at["fill", x] + 1)
                    copy_fill(nc.scalar.copy, x).then_inc(act_fill, 1)

            def pack(c):
                act.wait_ge(flipped, 2 * c + 1)
                for place in ACT_PLACES:
                    last = copy_pairs(nc.scalar.copy, c, 1, *place)
                last.then_inc(act_packed, 1)

            def tiles(c):
                wait(act, layer1, 2 * c)
                act.wait_ge(filled, fill_at["tiles", c] + 1)
                for k in range(KT):
                    last = nc.scalar.copy(packed_t[0:KSIZE[k], k, :], bank("tiles", c)[0:KSIZE[k], k, :])
                last.then_inc(tiles_copied, 1)

            def layer1_(c):
                wait(act, layer2, 2 * c)
                act.wait_ge(layer1, 2 * c + 2)
                for t in range(HALF, T1):
                    nc.scalar.activation(h1_sb[:, t, :], h1_ps(c, t), ACT.Relu,
                                         bias=b1_sb[:, t:t + 1]).then_inc(act_h1, 1)

            def layer2_(c):
                wait(act, layer3, c)
                act.wait_ge(layer2, T2 * c + 2)
                nc.scalar.activation(h2_sb[:, 1, :], h2_ps(c, 1), ACT.Relu, bias=b2_sb[:, 1:2]).then_inc(act_h2, 1)

            act.wait_ge(row_no_ready, 1)
            nc.scalar.activation(minus_row_no[:], row_no[:], ACT.Identity, scale=-1.0).then_inc(minus_row_no_ready, 1)
            act.wait_ge(minus_row_no_ready, 1)
            for k in range(AHEAD):
                distances(k)
                split(k)
                onehots(k)
            steps = {"whole": whole, "group": group, "fill": fill, "pack": pack, "tiles": tiles,
                     "layer1": layer1_, "layer2": layer2_}
            for n, (step, x) in enumerate(plan):
                if step == "fill" and x == (0, 0):
                    act.wait_ge(layer_in, LAYER_IN)
                if step in steps:
                    steps[step](x)


def kernel(**inputs):
    import numpy as np
    import concourse.bacc as bacc
    from concourse.bass_utils import run_bass_kernel_spmd

    a = {k: np.asarray(v) for k, v in inputs.items()}
    B, NF = a["ids"].shape
    order = slot_order([a[f"tbl_{f}"].shape[0] for f in range(NF)])
    ids = a["ids"][:, order].reshape(B // P, P // QUAD, QUAD, NF).transpose(0, 2, 1, 3).reshape(B // P, P, NF)
    n_dense = a["dense_ctx"].shape[1]
    places, n_packed = pair_places(NF, n_dense)
    n_rows = a["W_top1"].shape[0]
    w1 = np.zeros((-(-n_packed // P) * P, a["W_top1"].shape[1]), a["W_top1"].dtype)
    for first, at, width in places:
        for j in (first, first + 1):
            for i in range(j):
                lo, hi = sorted((order[i], order[j]))
                w1[at + (j - first) * width + i] = a["W_top1"][hi * (hi - 1) // 2 + lo]
    w1[:n_dense] = a["W_top1"][n_rows - n_dense:]
    arrays = {
        "dense": a["dense_ctx"],
        "ids": np.ascontiguousarray(np.concatenate([ids[0]] + [ids[c][:, WHOLE:] for c in range(1, B // P)], axis=1)),
        "ids_whole": np.ascontiguousarray(ids[1:, :, :WHOLE].transpose(2, 0, 1).reshape(WHOLE, B - P)),
        "w1": w1, "w2": a["W_top2"],
        "w3": np.ascontiguousarray(a["W_top3"].reshape(-1, P).T),
        "b1": np.ascontiguousarray(a["b_top1"].reshape(-1, P).T),
        "b2": np.ascontiguousarray(a["b_top2"].reshape(-1, P).T),
        **{f"tbl_{f}": a[f"tbl_{f}"] for f in range(NF)},
    }
    nc = bacc.Bacc("TRN2", target_bir_lowering=False, num_devices=1)
    ap = {k: nc.dram_tensor(f"in_{k}", v.shape, mybir.dt.from_np(v.dtype), kind="ExternalInput").ap()
          for k, v in arrays.items()}
    out = nc.dram_tensor("out_y", (B, 1), mybir.dt.float32, kind="ExternalOutput").ap()
    dlrm_tower_kernel(nc, ap["dense"], ap["ids"], ap["ids_whole"], [ap[f"tbl_{f}"] for f in order],
                      ap["w1"], ap["b1"], ap["w2"], ap["b2"], ap["w3"], out)
    r = run_bass_kernel_spmd(nc, [{f"in_{k}": v for k, v in arrays.items()}], core_ids=[0])
    return r.results[0]["out_y"]
```
